# Optimizing a Trainium2 kernel written in Bass

```python
import numpy as np
import jax
import jax.numpy as jnp

def _softmax(x, axis=-1):
    return jax.nn.softmax(x, axis=axis)

def _gelu(x):
    return jax.nn.gelu(x, approximate=True)

def _silu(x):
    return jax.nn.silu(x)

def _sigmoid(x):
    return jax.nn.sigmoid(x)

def _layernorm(x, axis=-1, eps=1e-05):
    m = jnp.mean(x, axis=axis, keepdims=True)
    v = jnp.var(x, axis=axis, keepdims=True)
    return (x - m) / jnp.sqrt(v + eps)

def _scatter_add(tgt, idx, src, axis=0):
    return tgt.at[idx].add(src)

def _segment_sum(src, seg, n):
    return jax.ops.segment_sum(src, seg, n)
kernel_name = 'mk_gnn_preln_d2_gnn_r8_ce3f2c'

def setup_inputs(seed: int=0):
    np.random.seed(seed)
    _w = jnp.asarray

    def _rec_inputs():
        import jax
        import jax.numpy as jnp
        _gk = jax.random.key(seed)
        x = -1.781e-05 + 1 * jax.random.normal(jax.random.fold_in(_gk, 1), (12500, 128), jnp.float32)
        src = jax.random.randint(jax.random.fold_in(_gk, 2), (400000,), 0, 12500, jnp.int32)
        dst = jax.random.randint(jax.random.fold_in(_gk, 3), (400000,), 0, 12500, jnp.int32)
        _o = jnp.argsort(dst, stable=True)
        src = src[_o]
        dst = dst[_o]
        edge_attr_96 = 5.93493e-05 + 1.00006 * jax.random.normal(jax.random.fold_in(_gk, 13), (400000, 96), jnp.float32)
        edge_type_201 = jax.random.randint(jax.random.fold_in(_gk, 15), (400000,), 0, 201, jnp.int32)
        return (x, src, dst, edge_attr_96, edge_type_201)
    x, src, dst, edge_attr_96, edge_type_201 = _rec_inputs()

    def _L0_gnn_setup():
        import jax, jax.numpy as jnp
        import numpy as np
        import math
        N = 12500
        IN = 128
        OUT = 128
        R = 200
        T = 62500
        E = 2 * T + N
        key = jax.random.key(seed)
        k = jax.random.split(key, 8)
        stdv = 1.0 / math.sqrt(OUT)
        src1 = jax.random.randint(k[0], (T,), 0, N, dtype=jnp.int32)
        dst1 = jax.random.randint(k[1], (T,), 0, N, dtype=jnp.int32)
        loops = jnp.arange(N, dtype=jnp.int32)
        src = jnp.concatenate([src1, dst1, loops])
        dst = jnp.concatenate([dst1, src1, loops])
        et1 = jax.random.randint(k[2], (T,), 1, R + 1, dtype=jnp.int32)
        et2 = jax.random.randint(k[3], (T,), 1, R + 1, dtype=jnp.int32)
        et_loop = jnp.full((N,), R, dtype=jnp.int32)
        all_edge_type = jnp.concatenate([et1, et2, et_loop])
        x = jax.random.normal(k[4], (N, IN), dtype=jnp.float32)
        weight = jax.random.uniform(k[5], (IN, OUT), jnp.float32, -stdv, stdv)
        bias = jax.random.uniform(k[6], (OUT,), jnp.float32, -stdv, stdv)
        alpha = jax.random.normal(k[7], (R + 1, 1), dtype=jnp.float32)
        alpha = alpha.at[0].set(0.0)
        return {'input': x, 'all_edge_type': all_edge_type, 'src': src, 'dst': dst, 'weight': weight, 'alpha': alpha, 'bias': bias}
    _L0_gnn_all = _L0_gnn_setup()
    _L0_gnn_in = {k: v for k, v in _L0_gnn_all.items() if k in ('weight', 'alpha', 'bias')}
    del _L0_gnn_all

    def _L1_gnn_setup():
        import jax, jax.numpy as jnp
        import numpy as np
        N_NODES = 6250
        N_EDGES = 100000
        NODE_DIM = 128
        EDGE_DIM = 96
        HIDDEN = 256
        N_GRAPHS = 16
        U_DIM = 64

        def scatter_mean(vals, idx, num_segments):
            s = jax.ops.segment_sum(vals, idx, num_segments=num_segments)
            cnt = jax.ops.segment_sum(jnp.ones((vals.shape[0],), vals.dtype), idx, num_segments=num_segments)
            return s / jnp.maximum(cnt, 1.0)[:, None]
        key = jax.random.key(seed)
        ks = jax.random.split(key, 16)
        glorot = lambda k, shp: jax.random.normal(k, shp, dtype=jnp.float32) * (2.0 / (shp[0] + shp[1])) ** 0.5
        return {'x': jax.random.normal(ks[0], (N_NODES, NODE_DIM), dtype=jnp.float32), 'edge_index': jax.random.randint(ks[1], (2, N_EDGES), 0, N_NODES, dtype=jnp.int64), 'edge_attr': jax.random.normal(ks[2], (N_EDGES, EDGE_DIM), dtype=jnp.float32), 'u': jax.random.normal(ks[3], (N_GRAPHS, U_DIM), dtype=jnp.float32), 'batch': jax.random.randint(ks[4], (N_NODES,), 0, N_GRAPHS, dtype=jnp.int64), 'W1': glorot(ks[5], (NODE_DIM + EDGE_DIM, HIDDEN)), 'b1': jnp.zeros((HIDDEN,), jnp.float32), 'W2': glorot(ks[6], (HIDDEN, HIDDEN)), 'b2': jnp.zeros((HIDDEN,), jnp.float32), 'Wa': glorot(ks[7], (HIDDEN, 1)), 'ba': jnp.zeros((1,), jnp.float32), 'W3': glorot(ks[8], (NODE_DIM + HIDDEN, HIDDEN)), 'b3': jnp.zeros((HIDDEN,), jnp.float32), 'W4': glorot(ks[9], (HIDDEN, NODE_DIM)), 'b4': jnp.zeros((NODE_DIM,), jnp.float32)}
    _L1_gnn_all = _L1_gnn_setup()
    _L1_gnn_in = {k: v for k, v in _L1_gnn_all.items() if k in ('u', 'W1', 'b1', 'W2', 'b2', 'Wa', 'ba', 'W3', 'b3', 'W4', 'b4')}
    del _L1_gnn_all
    return {'x': x, 'src': src, 'dst': dst, 'edge_attr_96': edge_attr_96, 'edge_type_201': edge_type_201, 'L0_gnn_weight': _L0_gnn_in['weight'], 'L0_gnn_alpha': _L0_gnn_in['alpha'], 'L0_gnn_bias': _L0_gnn_in['bias'], 'L1_gnn_u': _L1_gnn_in['u'], 'L1_gnn_W1': _L1_gnn_in['W1'], 'L1_gnn_b1': _L1_gnn_in['b1'], 'L1_gnn_W2': _L1_gnn_in['W2'], 'L1_gnn_b2': _L1_gnn_in['b2'], 'L1_gnn_Wa': _L1_gnn_in['Wa'], 'L1_gnn_ba': _L1_gnn_in['ba'], 'L1_gnn_W3': _L1_gnn_in['W3'], 'L1_gnn_b3': _L1_gnn_in['b3'], 'L1_gnn_W4': _L1_gnn_in['W4'], 'L1_gnn_b4': _L1_gnn_in['b4']}

def reference(x, src, dst, edge_attr_96, edge_type_201, L0_gnn_weight, L0_gnn_alpha, L0_gnn_bias, L1_gnn_u, L1_gnn_W1, L1_gnn_b1, L1_gnn_W2, L1_gnn_b2, L1_gnn_Wa, L1_gnn_ba, L1_gnn_W3, L1_gnn_b3, L1_gnn_W4, L1_gnn_b4):
    import jax
    import jax.numpy as jnp

    def _L0_gnn_ref(input, all_edge_type, src, dst, weight, alpha, bias):
        import jax, jax.numpy as jnp
        import numpy as np
        import math
        N = 12500
        IN = 128
        OUT = 128
        R = 200
        T = 62500
        E = 2 * T + N
        n = input.shape[0]
        e = all_edge_type.shape[0]
        t = (e - n) // 2
        tbl = alpha.at[0].set(0.0)
        feats = input @ weight
        t_et = jnp.concatenate([all_edge_type[t:2 * t], all_edge_type[:t], all_edge_type[-n:]])
        alp = tbl[all_edge_type] + tbl[t_et]
        msg = feats[src] * alp
        out = jax.ops.segment_sum(msg, dst, num_segments=n)
        return out + bias

    def _L1_gnn_ref(x, edge_index, edge_attr, u, batch, W1, b1, W2, b2, Wa, ba, W3, b3, W4, b4):
        import jax, jax.numpy as jnp
        import numpy as np
        N_NODES = 6250
        N_EDGES = 100000
        NODE_DIM = 128
        EDGE_DIM = 96
        HIDDEN = 256
        N_GRAPHS = 16
        U_DIM = 64

        def scatter_mean(vals, idx, num_segments):
            s = jax.ops.segment_sum(vals, idx, num_segments=num_segments)
            cnt = jax.ops.segment_sum(jnp.ones((vals.shape[0],), vals.dtype), idx, num_segments=num_segments)
            return s / jnp.maximum(cnt, 1.0)[:, None]
        row = edge_index[0]
        agg = scatter_mean(edge_attr, row, x.shape[0])
        h = jnp.concatenate([x, agg], axis=1)
        h = jax.nn.relu(h @ W1 + b1) @ W2 + b2
        attn = jax.nn.sigmoid(h @ Wa + ba)
        h = h * attn
        h = jnp.concatenate([x, h], axis=1)
        return jax.nn.relu(h @ W3 + b3) @ W4 + b4
    edge_index = jnp.stack([src, dst])
    batch0 = jnp.zeros((12500,), jnp.int32)
    h = jnp.maximum(_layernorm(x, axis=-1), 0.0)
    x = x + _L0_gnn_ref(h, edge_type_201, src, dst, L0_gnn_weight, L0_gnn_alpha, L0_gnn_bias)
    h = jnp.maximum(_layernorm(x, axis=-1), 0.0)
    x = x + _L1_gnn_ref(h, edge_index, edge_attr_96, L1_gnn_u, batch0, L1_gnn_W1, L1_gnn_b1, L1_gnn_W2, L1_gnn_b2, L1_gnn_Wa, L1_gnn_ba, L1_gnn_W3, L1_gnn_b3, L1_gnn_W4, L1_gnn_b4)
    return x

_drawn_inputs = setup_inputs


def setup_inputs(seed=0):
    import zlib

    import numpy as np

    out = dict(_drawn_inputs(seed))
    spreads = {'L1_gnn_b1': (0.0, 0.8),
     'L1_gnn_b2': (0.0, 0.735),
     'L1_gnn_b3': (0.0, 0.349),
     'L1_gnn_b4': (0.0, 0.278)}
    factors = {'edge_attr_96': 7.443, 'L0_gnn_bias': 3.946, 'L1_gnn_Wa': 7.659}
    for name, (base, spread) in spreads.items():
        noise = np.random.default_rng([zlib.crc32(name.encode()), seed]).standard_normal(out[name].shape)
        drawn = base * np.exp(spread * noise) if base else spread * noise
        out[name] = jnp.asarray(drawn.astype(out[name].dtype))
    for name, factor in factors.items():
        out[name] = (out[name] * factor).astype(out[name].dtype)
    return out
```

```python
import concourse.bass as bass
from concourse import mybir
from contextlib import ExitStack


def gnn_program(nc, x, src, dst, edge_attr_96, edge_type_201, L0_gnn_weight, L0_gnn_alpha, L0_gnn_bias,
                L1_gnn_W1, L1_gnn_b1, L1_gnn_W2, L1_gnn_b2, L1_gnn_Wa, L1_gnn_ba,
                L1_gnn_W3, L1_gnn_b3, L1_gnn_W4, L1_gnn_b4, out):
    fp32, bf16, i32 = mybir.dt.float32, mybir.dt.bfloat16, mybir.dt.int32
    ALU, ACT, AX = mybir.AluOpType, mybir.ActivationFunctionType, mybir.AxisListType
    ds = bass.ds

    N, D = x.shape
    E, FE = edge_attr_96.shape
    R1 = L0_gnn_alpha.shape[0]
    HID = L1_gnn_W1.shape[1]
    T = (E - N) // 2
    P = 128
    J = 25
    Q = 5
    SB = P * J
    NS = E // SB
    NQ = J // Q
    TN = N // NS
    FC = FE + 1
    NT = 99 * P
    W = 128
    WG = 512
    NWG = 25
    AC = NWG * WG
    LAG = 2
    assert NS * SB == E and NS * TN == N and NT >= N + P and AC >= N + W and Q * NQ == J
    MH = HID // P
    EPS = 1e-5

    ctx = ExitStack()
    with ctx:
        def sb(name, shape, dt=fp32):
            return ctx.enter_context(nc.sbuf_tensor(name, shape, dt))

        def sem(name):
            return ctx.enter_context(nc.semaphore(name))

        tables = [nc.dram_tensor(f"attr_sums_{k}", (NT, FC), fp32) for k in range(Q)]
        feats_d = nc.dram_tensor("feats_d", (N, D), fp32)
        vswap_d = nc.dram_tensor("vswap_d", (E,), fp32)

        ident = sb("ident", [P, P])
        identb = sb("identb", [P, P], bf16)
        later = sb("later", [P, P])
        iota_f = sb("iota_f", [P, WG])
        ones_col = sb("ones_col", [P, 1])
        spare_row = sb("spare_row", [P, 1])
        alpha_row = sb("alpha_row", [P, R1])
        w0 = sb("w0", [D, D])
        bias0 = sb("bias0", [D, 1])
        w1x = sb("w1x", [P, HID])
        w1a = sb("w1a", [FE, HID])
        w2 = sb("w2", [P, MH, HID])
        wa = sb("wa", [P, MH])
        wab = sb("wab", [P, MH, P])
        w3 = sb("w3", [P, 1 + MH, HID])
        w4 = sb("w4", [P, MH, D])
        b1 = sb("b1", [P, MH])
        b2 = sb("b2", [P, MH])
        b3 = sb("b3", [P, MH])
        b4 = sb("b4", [P, 1])
        ba = sb("ba", [P, 1])

        src_all = sb("src_all", [P, NS * J], i32)
        dst_then_v = sb("dst_then_v", [P, NS * J], i32)
        type_then_vswap = sb("type_then_vswap", [P, NS * J], i32)
        dst_all, v_all = dst_then_v[:, :], dst_then_v[:, :].bitcast(fp32)
        type_all, vswap_all = type_then_vswap[:, :], type_then_vswap[:, :].bitcast(fp32)
        dstrel_all = sb("dstrel_all", [P, NS * J])
        base_i = sb("base_i", [P, NS], i32)
        acc = sb("acc", [P, AC])

        attr = sb("attr", [P, NQ, Q * FE])
        stage = sb("stage", [P, J, FC])
        same = sb("same", [P, Q, P])
        later_n = sb("later_n", [P, J])
        src_i2 = sb("src_i2", [P, 2, J], i32)
        src_hl = sb("src_hl", [P, 2, J], bf16)
        src_f = sb("src_f", [P, J])
        src_off = sb("src_off", [P, J])
        pick = sb("pick", [P, J])
        idx_b = sb("idx_b", [P, J], i32)
        type_f = sb("type_f", [P, J])
        v_t = sb("v_t", [P, J])
        junk = sb("junk", [P, Q, R1], bf16)
        x_t = sb("x_t", [TN, D])
        bn6 = sb("bn6", [TN, 6])
        mv = sb("mv", [TN, 2])
        var_eps = sb("var_eps", [TN, 1])
        std = sb("std", [TN, 1])
        rstd = sb("rstd", [TN, 1])
        nbias = sb("nbias", [TN, 1])
        h_t = sb("h_t", [TN, D])
        hT = sb("hT", [D, TN])
        f_t = sb("f_t", [TN, D])

        gath = sb("gath", [P, J, D])
        onehot = sb("onehot", [P, Q, WG])
        idx_a = sb("idx_a", [P, J], i32)
        rel_t = sb("rel_t", [P, J])
        alp_t = sb("alp_t", [P, J])
        tab_t = sb("tab_t", [TN, Q, FC])
        acc_t = sb("acc_t", [P, TN])
        x1_t = sb("x1_t", [TN, D])
        asum = sb("asum", [TN, FC])
        cnt1 = sb("cnt1", [TN, 1])
        rcnt = sb("rcnt", [TN, 1])
        agg_t = sb("agg_t", [TN, FE])
        aT = sb("aT", [FE, TN])
        z1 = sb("z1", [P, MH, TN])
        z2 = sb("z2", [P, MH, TN])
        att = sb("att", [P, TN])
        h2 = sb("h2", [P, MH, TN])
        z3 = sb("z3", [P, MH, TN])
        yT = sb("yT", [P, TN])
        y_t = sb("y_t", [TN, D])

        bank = [ctx.enter_context(nc.psum_tensor(f"bank{k}", [P, 512], fp32)) for k in range(8)]

        PART_END = {0: 3, 3: Q}

        def ring5(b, k, n):
            return bank[b][:, k * P:k * P + n] if k < 3 else bank[b + 1][:, (k - 3) * P:(k - 3) * P + n]

        s_edges = sem("s_edges")
        s_wts = sem("s_wts")
        s_zero = sem("s_zero")
        s_const = sem("s_const")
        s_prep = sem("s_prep")
        s_dstrel = sem("s_dstrel")
        s_attr = [sem(f"s_attr{q}") for q in range(NQ)]
        s_meta = sem("s_meta")
        s_metaf = sem("s_metaf")
        s_row = sem("s_row")
        s_same = sem("s_same")
        s_sum = sem("s_sum")
        s_stage = sem("s_stage")
        s_pick = sem("s_pick")
        s_idx = sem("s_idx")
        s_tab = [sem(f"s_tab{k}") for k in range(Q)]
        s_look = sem("s_look")
        s_v = sem("s_v")
        s_vst = sem("s_vst")
        s_x = sem("s_x")
        s_bn = sem("s_bn")
        s_std = sem("s_std")
        s_norm = sem("s_norm")
        s_h = sem("s_h")
        s_hp = sem("s_hp")
        s_hT = sem("s_hT")
        s_fp = sem("s_fp")
        s_f = sem("s_f")
        s_fst = sem("s_fst")
        s_ffree = sem("s_ffree")
        s_vsw = sem("s_vsw")
        s_idxa = sem("s_idxa")
        s_gath = [sem(f"s_gath{j}") for j in range(J)]
        s_alp = sem("s_alp")
        s_oh = sem("s_oh")
        s_mm = sem("s_mm")
        s_flush = sem("s_flush")
        s_tload = sem("s_tload")
        s_acct = sem("s_acct")
        s_accp = sem("s_accp")
        s_x1 = sem("s_x1")
        s_nrm2 = sem("s_nrm2")
        s_std2 = sem("s_std2")
        s_h1 = sem("s_h1")
        s_agg = sem("s_agg")
        s_tp = sem("s_tp")
        s_tT = sem("s_tT")
        s_z1p = sem("s_z1p")
        s_z1 = sem("s_z1")
        s_z2p = sem("s_z2p")
        s_z2 = sem("s_z2")
        s_lp = sem("s_lp")
        s_att = sem("s_att")
        s_h2 = sem("s_h2")
        s_z3p = sem("s_z3p")
        s_z3 = sem("s_z3")
        s_yp = sem("s_yp")
        s_yT = sem("s_yT")
        s_yt = sem("s_yt")
        s_y = sem("s_y")
        s_out = sem("s_out")
        s_yfree = sem("s_yfree")

        N_EDGES = 64
        block = ctx.enter_context(nc.Block())

        @block.sync
        def _(sp):
            v = lambda a: a.rearrange("(s p j) -> p s j", p=P, j=J)
            all3 = lambda t: t.rearrange("p (s j) -> p s j", j=J)
            sp.dma_start(all3(src_all[:, :]), v(src)).then_inc(s_edges, 16)
            sp.dma_start(all3(type_all), v(edge_type_201)).then_inc(s_edges, 16)
            sp.dma_start(all3(dst_all), v(dst)).then_inc(s_edges, 16)
            with nc.allow_non_contiguous_dma(reason="one index per superblock"):
                sp.dma_start(base_i[:, :], bass.AP(dst.tensor, 0, [[0, P], [SB, NS], [1, 1]])).then_inc(s_edges, 16)
            attr_v = edge_attr_96.rearrange("(s p j) f -> s p (j f)", p=P, j=J)
            x_v = x.rearrange("(t n) f -> t n f", n=TN)
            feats_v = feats_d.rearrange("(t n) f -> t n f", n=TN)

            def loads_b(s, first=False):
                for q in range(NQ):
                    if not first:
                        sp.wait_ge(s_sum, J + J * (s - 1) + Q * (q + 1))
                    sp.dma_start(attr[:, q, :], attr_v[ds(s, 1), :, q * Q * FE:(q + 1) * Q * FE].rearrange(
                        "o p f -> (o p) f")).then_inc(s_attr[q], 16)
                    if q == 0:
                        sp.wait_ge(s_h, 1 + s)
                        sp.dma_start(x_t[:, :], x_v[ds(s, 1), :, :].rearrange("o n f -> (o n) f")).then_inc(s_x, 16)

            def store_f(s):
                sp.wait_ge(s_f, s + 2)
                sp.dma_start(feats_v[ds(s, 1), :, :].rearrange("o n f -> (o n) f"), f_t[:, :]).then_inc(s_fst, 16)
                sp.wait_ge(s_fst, 16 * (s + 1))
                sp.sem_inc(s_ffree, 1)

            def store_v(s, p0, p1, shift):
                sp.wait_ge(s_v, s + 1)
                dest = vswap_d[ds(s * SB + p0 * J + shift, (p1 - p0) * J)].rearrange("(p j) -> p j", j=J)
                sp.dma_start(dest, v_all[p0:p1, ds(s * J, J)]).then_inc(s_vst, 16)

            sp.sem_inc(s_ffree, 1)
            sp.wait_ge(s_h, 1)
            loads_b(0, first=True)
            cut1, cut2 = T // SB, 2 * T // SB
            pc1, pc2 = (T - cut1 * SB) // J, (2 * T - cut2 * SB) // J
            assert cut1 * SB + pc1 * J == T and cut2 * SB + pc2 * J == 2 * T
            spans = [(0, cut1, [(0, P, T)]), (cut1, cut1 + 1, [(0, pc1, T), (pc1, P, -T)]),
                     (cut1 + 1, cut2, [(0, P, -T)]), (cut2, cut2 + 1, [(0, pc2, -T), (pc2, P, 0)]),
                     (cut2 + 1, NS, [(0, P, 0)])]
            n_vst = 0
            for lo, hi, parts in spans:
                n_vst += (hi - lo) * len(parts)
                with sp.Fori(lo, hi if hi < NS else NS - 1) as s:
                    loads_b(s + 1)
                    store_f(s)
                    for p0, p1, shift in parts:
                        store_v(s, p0, p1, shift)
            store_f(NS - 1)
            store_v(NS - 1, 0, P, 0)

            sp.wait_ge(s_vst, 16 * n_vst)
            sp.dma_start(all3(vswap_all), v(vswap_d)).then_inc(s_vsw, 16)
            for k in range(Q):
                sp.wait_ge(s_tab[k], 16 * NQ + 16 * NS * NQ)
            sp.sem_inc(s_yfree, 1)
            with sp.Fori(0, NS) as t:
                sp.wait_ge(s_y, t + 1)
                sp.dma_start(x_t[:, :], x_v[ds(t, 1), :, :].rearrange("o n f -> (o n) f")).then_inc(s_tload, 16)
                for k in range(Q):
                    sp.dma_start(tab_t[:, k, :], tables[k][ds(t * TN, TN), :]).then_inc(s_tload, 16)
                sp.wait_ge(s_y, t + 2)
                sp.dma_start(out[ds(t * TN, TN), :], y_t[:, :]).then_inc(s_out, 16)
                sp.wait_ge(s_out, 16 * (t + 1))
                sp.sem_inc(s_yfree, 1)
            sp.wait_ge(s_out, 16 * NS)

        @block.gpsimd
        def _(gp):
            gp.memset(ident[:, :], 0.0).then_inc(s_const, 1)
            gp.memset(later[:, :], 1.0).then_inc(s_const, 1)
            gp.wait_ge(s_const, 2)
            gp.affine_select(out=ident[:, :], in_=ident[:, :], compare_op=ALU.not_equal, fill=1.0, base=0,
                             pattern=[[-1, P]], channel_multiplier=1).then_inc(s_const, 1)
            gp.affine_select(out=later[:, :], in_=later[:, :], compare_op=ALU.is_ge, fill=0.0, base=0,
                             pattern=[[1, P]], channel_multiplier=-1).then_inc(s_const, 1)
            gp.iota(iota_f[:, :], pattern=[[1, WG]], base=0, channel_multiplier=0,
                    allow_small_or_imprecise_dtypes=True).then_inc(s_const, 1)
            gp.iota(spare_row[:, :], pattern=[[0, 1]], base=N, channel_multiplier=1,
                    allow_small_or_imprecise_dtypes=True).then_inc(s_const, 1)

            gp.wait_ge(s_zero, 1)
            rows = NT // P
            for n in range(NQ):
                a0, a1 = n * rows // NQ, (n + 1) * rows // NQ
                for k in range(Q):
                    if n:
                        gp.wait_ge(s_tab[k], 16 * n)
                    gp.dma_start(tables[k].rearrange("(p a) f -> p (a f)", p=P)[:, a0 * FC:a1 * FC],
                                 acc[:, 0:(a1 - a0) * FC]).then_inc(s_tab[k], 16)
            with gp.Fori(0, NS) as s:
                for q in range(NQ):
                    gp.wait_ge(s_idx, NQ * s + q + 1)
                    gp.nop(nofuse=True)
                    for k in range(Q):
                        j = q * Q + k
                        gp.wait_ge(s_tab[k], 16 * NQ + 16 * (NQ * s + q))
                        gp.nop(nofuse=True)
                        gp.indirect_dma_start(tables[k][:, :], bass.IndirectOffsetOnAxis(ap=idx_b[:, j:j + 1], axis=0),
                                              stage[:, j, :], None, compute_op=ALU.add).then_inc(s_tab[k], 16)
            gp.wait_ge(s_fst, 16 * NS)
            gp.nop(nofuse=True)
            with gp.Fori(0, NS) as s:
                for q in range(NQ):
                    gp.wait_ge(s_idxa, NQ * s + q + 1)
                    gp.nop(nofuse=True)
                    for k in range(Q):
                        j = q * Q + k
                        gp.indirect_dma_start(gath[:, j, :], None, feats_d[:, :],
                                              bass.IndirectOffsetOnAxis(ap=idx_a[:, j:j + 1], axis=0)
                                              ).then_inc(s_gath[j], 16)

        @block.tensor
        def _(pe):
            pe.sem_inc(s_sum, J)
            pe.sem_inc(s_mm, J)
            pe.wait_ge(s_prep, 1)
            pe.wait_ge(s_wts, 16 * N_WTS)

            with pe.Fori(0, NS) as s:
                for q in range(NQ):
                    for k in range(Q):
                        j = q * Q + k
                        if j == 0:
                            pe.wait_ge(s_meta, s + 1)
                        if k in PART_END:
                            pe.wait_ge(s_same, J * s + q * Q + PART_END[k])
                        for half in range(2):
                            last = nc.tensor.matmul(ring5(0, k, P), src_hl[:, half, j:j + 1].to_broadcast([P, P]),
                                                    identb[:, :], start=half == 0, stop=half == 1)
                        last.then_inc(s_row, 1)
                    pe.wait_ge(s_attr[q], 16 * (s + 1))
                    for k in range(Q):
                        j = q * Q + k
                        pe.wait_ge(s_same, Q + J * s + j + 1)
                        if k in PART_END:
                            pe.wait_ge(s_stage, J * s + q * Q + PART_END[k])
                        ps = ring5(2, k, FC)
                        nc.tensor.matmul(ps[:, 0:FE], same[:, k, :], attr[:, q, k * FE:(k + 1) * FE],
                                         start=True, stop=True)
                        nc.tensor.matmul(ps[:, FE:FC], same[:, k, :], ones_col[:, :],
                                         start=True, stop=True).then_inc(s_sum, 1)
                    if q == 2:
                        pe.wait_ge(s_h, s + 2)
                        nc.tensor.transpose(bank[5][:, 0:TN], h_t[:, :], ident[0:TN, 0:TN]).then_inc(s_hp, 1)
                    if q == 3:
                        pe.wait_ge(s_hT, s + 1)
                        pe.wait_ge(s_f, s + 1)
                        nc.tensor.matmul(bank[6][0:TN, 0:D], hT[:, :], w0[:, :], start=True, stop=True
                                         ).then_inc(s_fp, 1)

            def sums(s, q):
                for k in range(Q):
                    j = q * Q + k
                    if j == 0:
                        pe.wait_ge(s_flush, s + 1)
                    pe.wait_ge(s_gath[j], 16 * (s + 1))
                    pe.wait_ge(s_oh, J * s + j + 1)
                    nc.tensor.matmul(bank[4][:, 0:W], gath[:, j, :], onehot[:, k, 0:W],
                                     start=j == 0, stop=j == J - 1).then_inc(s_mm, 1)

            def net(t, part):
                if part == 0:
                    pe.wait_ge(s_acct, t + 1)
                    nc.tensor.transpose(bank[0][0:TN, 0:D], acc_t[:, :], ident[:, :]).then_inc(s_accp, 1)
                if part == 1:
                    pe.wait_ge(s_h1, t + 1)
                    nc.tensor.transpose(bank[0][:, 128:128 + TN], h_t[:, :], ident[0:TN, 0:TN])
                    pe.wait_ge(s_agg, 4 * (t + 1))
                    nc.tensor.transpose(bank[0][0:FE, 256:256 + TN], agg_t[:, :], ident[0:TN, 0:TN]).then_inc(s_tp, 1)
                    pe.wait_ge(s_tT, 2 * (t + 1))
                    for m in range(MH):
                        col = slice(m * P, (m + 1) * P)
                        nc.tensor.matmul(bank[1][:, m * P:m * P + TN], w1x[:, col], hT[:, :], start=True, stop=False)
                        last = nc.tensor.matmul(bank[1][:, m * P:m * P + TN], w1a[:, col], aT[:, :],
                                                start=False, stop=True)
                    last.then_inc(s_z1p, 1)
                if part == 2:
                    pe.wait_ge(s_z1, MH * (t + 1))
                    for m in range(MH):
                        for c in range(MH):
                            last = nc.tensor.matmul(bank[2][:, m * P:m * P + TN], w2[:, c, m * P:(m + 1) * P],
                                                    z1[:, c, :], start=c == 0, stop=c == MH - 1)
                    last.then_inc(s_z2p, 1)
                    pe.wait_ge(s_z2, MH * (t + 1))
                    for c in range(MH):
                        last = nc.tensor.matmul(bank[3][:, 0:TN], wab[:, c, :], z2[:, c, :],
                                                start=c == 0, stop=c == MH - 1)
                    last.then_inc(s_lp, 1)
                if part == 3:
                    pe.wait_ge(s_h2, t + 1)
                    for m in range(MH):
                        for c in range(1 + MH):
                            last = nc.tensor.matmul(bank[5][:, m * P:m * P + TN], w3[:, c, m * P:(m + 1) * P],
                                                    hT[:, :] if c == 0 else h2[:, c - 1, :],
                                                    start=c == 0, stop=c == MH)
                    last.then_inc(s_z3p, 1)
                    pe.wait_ge(s_z3, MH * (t + 1))
                    for c in range(MH):
                        last = nc.tensor.matmul(bank[6][:, 0:TN], w4[:, c, :], z3[:, c, :],
                                                start=c == 0, stop=c == MH - 1)
                    last.then_inc(s_yp, 1)
                if part == 4:
                    pe.wait_ge(s_yT, t + 1)
                    nc.tensor.transpose(bank[7][0:TN, 0:D], yT[:, :], ident[:, :]).then_inc(s_yt, 1)

            def superblock(s, with_net):
                for q in range(NQ):
                    sums(s, q)
                    if with_net:
                        net(s - LAG, q)

            with pe.Fori(0, LAG) as s:
                superblock(s, False)
            with pe.Fori(LAG, NS) as s:
                superblock(s, True)
            with pe.Fori(NS - LAG, NS) as t:
                for part in range(5):
                    net(t, part)

        @block.scalar
        def _(act):
            act.sem_inc(s_h, 1)
            act.sem_inc(s_f, 1)
            act.sem_inc(s_stage, Q)
            with nc.allow_non_contiguous_dma(reason="small parameter columns"):
                act.dma_start(alpha_row[:, :], bass.AP(L0_gnn_alpha.tensor, 0, [[0, P], [1, R1]])).then_inc(s_wts, 16)
                act.dma_start(w0[:, :], L0_gnn_weight).then_inc(s_wts, 16)
                act.dma_start(bias0[:, :], L0_gnn_bias.rearrange("(p o) -> p o", o=1)).then_inc(s_wts, 16)
                act.dma_start(w1x[:, :], L1_gnn_W1[0:D, :]).then_inc(s_wts, 16)
                act.dma_start(w1a[:, :], L1_gnn_W1[D:D + FE, :]).then_inc(s_wts, 16)
                act.dma_start(w2[:, :, :], L1_gnn_W2.rearrange("(c p) n -> p c n", p=P)).then_inc(s_wts, 16)
                act.dma_start(w3[:, :, :], L1_gnn_W3.rearrange("(c p) n -> p c n", p=P)).then_inc(s_wts, 16)
                act.dma_start(w4[:, :, :], L1_gnn_W4.rearrange("(c p) n -> p c n", p=P)).then_inc(s_wts, 16)
                act.dma_start(wa[:, :], L1_gnn_Wa.rearrange("(c p) o -> p (c o)", p=P)).then_inc(s_wts, 16)
                act.dma_start(b1[:, :], L1_gnn_b1.rearrange("(c p) -> p c", p=P)).then_inc(s_wts, 16)
                act.dma_start(b2[:, :], L1_gnn_b2.rearrange("(c p) -> p c", p=P)).then_inc(s_wts, 16)
                act.dma_start(b3[:, :], L1_gnn_b3.rearrange("(c p) -> p c", p=P)).then_inc(s_wts, 16)
                act.dma_start(b4[:, :], L1_gnn_b4.rearrange("(p o) -> p o", o=1)).then_inc(s_wts, 16)
                act.dma_start(ba[:, :], bass.AP(L1_gnn_ba.tensor, 0, [[0, P], [1, 1]])).then_inc(s_wts, 16)
            act.wait_ge(s_wts, 16 * N_WTS)

            with act.Fori(0, NS) as s:
                for q in range(NQ):
                    for k in range(Q):
                        j = q * Q + k
                        if k in PART_END:
                            act.wait_ge(s_sum, J + J * s + q * Q + PART_END[k])
                        act.wait_ge(s_tab[k], 16 * (NQ * s + q + 1))
                        nc.scalar.activation(stage[:, j, :], ring5(2, k, FC), ACT.Copy).then_inc(s_stage, 1)
                    if q == 0:
                        act.wait_ge(s_bn, 4 * s + 3)
                        nc.scalar.activation(std[:, :], var_eps[:, :], ACT.Sqrt).then_inc(s_std, 1)
                    if q == 1:
                        act.wait_ge(s_norm, s + 1)
                        nc.scalar.activation(h_t[:, :], x_t[:, :], ACT.Relu, bias=nbias[:, :], scale=rstd[:, :]
                                             ).then_inc(s_h, 1)
                    if q == 2:
                        act.wait_ge(s_hp, s + 1)
                        nc.scalar.activation(hT[:, :], bank[5][:, 0:TN], ACT.Copy).then_inc(s_hT, 1)
                    if q == 4:
                        act.wait_ge(s_fp, s + 1)
                        act.wait_ge(s_ffree, s + 1)
                        nc.scalar.activation(f_t[:, :], bank[6][0:TN, 0:D], ACT.Copy).then_inc(s_f, 1)

            def indices(s):
                for q in range(NQ):
                    act.wait_ge(s_mm, J * s + Q * (q + 1))
                    nc.scalar.activation(idx_a[:, q * Q:(q + 1) * Q], src_all[:, ds(s * J + q * Q, Q)], ACT.Copy
                                         ).then_inc(s_idxa, 1)

            def net(t):
                act.wait_ge(s_nrm2, 5 * t + 3)
                nc.scalar.activation(std[:, :], var_eps[:, :], ACT.Sqrt).then_inc(s_std2, 1)
                act.wait_ge(s_nrm2, 5 * (t + 1))
                nc.scalar.activation(h_t[:, :], x1_t[:, :], ACT.Relu, bias=nbias[:, :], scale=rstd[:, :]
                                     ).then_inc(s_h1, 1)
                act.wait_ge(s_tp, t + 1)
                nc.scalar.activation(hT[:, :], bank[0][:, 128:128 + TN], ACT.Copy).then_inc(s_tT, 1)
                nc.scalar.activation(aT[:, :], bank[0][0:FE, 256:256 + TN], ACT.Copy).then_inc(s_tT, 1)
                act.wait_ge(s_z1p, t + 1)
                for m in range(MH):
                    nc.scalar.activation(z1[:, m, :], bank[1][:, m * P:m * P + TN], ACT.Relu, bias=b1[:, m:m + 1]
                                         ).then_inc(s_z1, 1)
                act.wait_ge(s_z2p, t + 1)
                for m in range(MH):
                    nc.scalar.activation(z2[:, m, :], bank[2][:, m * P:m * P + TN], ACT.Identity, bias=b2[:, m:m + 1]
                                         ).then_inc(s_z2, 1)
                act.wait_ge(s_lp, t + 1)
                nc.scalar.activation(att[:, :], bank[3][:, 0:TN], ACT.Sigmoid, bias=ba[:, :]).then_inc(s_att, 1)
                act.wait_ge(s_z3p, t + 1)
                for m in range(MH):
                    nc.scalar.activation(z3[:, m, :], bank[5][:, m * P:m * P + TN], ACT.Relu, bias=b3[:, m:m + 1]
                                         ).then_inc(s_z3, 1)
                act.wait_ge(s_yp, t + 1)
                nc.scalar.activation(yT[:, :], bank[6][:, 0:TN], ACT.Identity, bias=b4[:, :]).then_inc(s_yT, 1)

            with act.Fori(0, LAG) as s:
                indices(s)
            with act.Fori(LAG, NS) as s:
                indices(s)
                net(s - LAG)
            with act.Fori(NS - LAG, NS) as t:
                net(t)

        @block.vector
        def _(dve):
            dve.sem_inc(s_same, Q)
            dve.sem_inc(s_look, 1)
            dve.sem_inc(s_flush, 1)
            nc.vector.memset(acc[:, :], 0.0).then_inc(s_zero, 1)
            nc.vector.memset(ones_col[:, :], 1.0)
            dve.wait_ge(s_wts, 16 * N_WTS)
            nc.vector.memset(alpha_row[:, 0:1], 0.0)
            for c in range(MH):
                nc.vector.tensor_copy(wab[:, c, :], wa[:, c:c + 1].to_broadcast([P, P]))
            dve.wait_ge(s_const, 6)
            nc.vector.tensor_copy(identb[:, :], ident[:, :]).then_inc(s_prep, 1)
            dve.wait_ge(s_edges, N_EDGES)
            nc.vector.tensor_tensor(dstrel_all[:, :].rearrange("p (s j) -> p s j", j=J),
                                    dst_all.rearrange("p (s j) -> p s j", j=J),
                                    base_i[:, :].unsqueeze(2).to_broadcast([P, NS, J]), ALU.subtract
                                    ).then_inc(s_dstrel, 1)
            dve.wait_ge(s_dstrel, 1)

            with dve.Fori(0, NS) as s:
                nc.vector.tensor_scalar(src_i2[:, 0, :], src_all[:, ds(s * J, J)], 0x7F80, None, ALU.bitwise_and
                                        ).then_inc(s_metaf, 1)
                nc.vector.tensor_scalar(src_i2[:, 1, :], src_all[:, ds(s * J, J)], 0x7F, None, ALU.bitwise_and
                                        ).then_inc(s_metaf, 1)
                nc.vector.tensor_copy(src_f[:, :], src_all[:, ds(s * J, J)]).then_inc(s_metaf, 1)
                nc.vector.tensor_copy(type_f[:, :], type_all[:, ds(s * J, J)]).then_inc(s_metaf, 1)
                dve.wait_ge(s_metaf, 4 * (s + 1))
                nc.vector.tensor_copy(src_hl[:, :, :], src_i2[:, :, :]).then_inc(s_meta, 1)
                nc.vector.tensor_scalar(src_off[:, :], src_f[:, :], spare_row[:, 0:1], None, ALU.subtract
                                        ).then_inc(s_pick, 1)
                for q in range(NQ):
                    group = slice(q * Q, (q + 1) * Q)
                    for k in range(Q):
                        j = q * Q + k
                        if k in PART_END:
                            dve.wait_ge(s_row, J * s + q * Q + PART_END[k])
                        dve.wait_ge(s_sum, J - Q + J * s + j + 1)
                        nc.vector.scalar_tensor_tensor(same[:, k, :], ring5(0, k, P), src_f[:, j:j + 1],
                                                       later[:, :], ALU.is_equal, ALU.mult,
                                                       accum_out=later_n[:, j:j + 1]).then_inc(s_same, 1)
                    for k in range(Q):
                        j = q * Q + k
                        if k == 0:
                            dve.wait_ge(s_look, NQ * s + q + 1)
                        last = nc.vector.scalar_tensor_tensor(junk[:, k, :], iota_f[:, 0:R1], type_f[:, j:j + 1],
                                                              alpha_row[:, :], ALU.is_equal, ALU.mult,
                                                              accum_out=v_t[:, j:j + 1])
                    last.then_inc(s_look, 1)
                    dve.wait_ge(s_same, Q + J * s + Q * (q + 1))
                    dve.wait_ge(s_pick, (NQ + 1) * s + q + 1)
                    nc.vector.scalar_tensor_tensor(pick[:, group], later_n[:, group], 1.0, src_off[:, group],
                                                   ALU.is_equal, ALU.mult).then_inc(s_pick, 1)
                    dve.wait_ge(s_pick, (NQ + 1) * s + q + 2)
                    dve.wait_ge(s_stage, Q + J * s + Q * (q + 1))
                    nc.vector.tensor_scalar(idx_b[:, group], pick[:, group], spare_row[:, 0:1], None, ALU.add
                                            ).then_inc(s_idx, 1)
                    if q == 0:
                        dve.wait_ge(s_x, 16 * (s + 1))
                        nc.vector.bn_stats(bn6[:, :], x_t[:, :]).then_inc(s_bn, 1)
                        dve.wait_ge(s_bn, 4 * s + 1)
                        dve.nop(nofuse=True)
                        nc.vector.bn_aggr(mv[:, :], bn6[:, :]).then_inc(s_bn, 1)
                        dve.wait_ge(s_bn, 4 * s + 2)
                        nc.vector.tensor_scalar(var_eps[:, :], mv[:, 1:2], EPS, None, ALU.add).then_inc(s_bn, 1)
                    if q == 1:
                        dve.wait_ge(s_std, s + 1)
                        nc.vector.reciprocal(rstd[:, :], std[:, :]).then_inc(s_bn, 1)
                        dve.wait_ge(s_bn, 4 * s + 4)
                        nc.vector.scalar_tensor_tensor(nbias[:, :], mv[:, 0:1], -1.0, rstd[:, :], ALU.mult, ALU.mult
                                                       ).then_inc(s_norm, 1)
                dve.wait_ge(s_look, NQ * (s + 1) + 1)
                nc.vector.tensor_copy(v_all[:, ds(s * J, J)], v_t[:, :]).then_inc(s_v, 1)

            dve.sem_inc(s_y, 1)
            dve.wait_ge(s_vsw, 16)

            def onehots(s, q):
                if q == 0:
                    nc.vector.tensor_copy(rel_t[:, :], dstrel_all[:, ds(s * J, J)]).then_inc(s_alp, 1)
                    nc.vector.tensor_tensor(alp_t[:, :], v_all[:, ds(s * J, J)], vswap_all[:, ds(s * J, J)], ALU.add
                                            ).then_inc(s_alp, 1)
                    dve.wait_ge(s_alp, 2 * (s + 1))
                for k in range(Q):
                    j = q * Q + k
                    dve.wait_ge(s_mm, J - Q + J * s + j + 1)
                    nc.vector.tensor_scalar(onehot[:, k, 0:W], iota_f[:, 0:W], rel_t[:, j:j + 1], alp_t[:, j:j + 1],
                                            ALU.is_equal, ALU.mult).then_inc(s_oh, 1)

            def flush(s):
                dve.wait_ge(s_mm, J + J * (s + 1))
                base = dve.value_load(base_i[0:1, ds(s, 1)], min_val=0, max_val=N - 1)
                nc.vector.tensor_tensor(acc[:, ds(base, W)], acc[:, ds(base, W)], bank[4][:, 0:W], ALU.add
                                        ).then_inc(s_flush, 1)

            def net(t, part, flushed):
                if part == 0:
                    dve.wait_ge(s_flush, flushed + 1)
                    nc.vector.tensor_scalar(acc_t[:, :], acc[:, ds(t * TN, TN)], bias0[:, 0:1], None, ALU.add
                                            ).then_inc(s_acct, 1)
                    dve.wait_ge(s_tload, 16 * (Q + 1) * (t + 1))
                    nc.vector.tensor_reduce(asum[:, :], tab_t[:, :, :].rearrange("p k f -> p f k"), AX.X, ALU.add
                                            ).then_inc(s_agg, 1)
                    dve.wait_ge(s_agg, 4 * t + 1)
                    nc.vector.tensor_scalar(cnt1[:, :], asum[:, FE:FC], 1.0, None, ALU.max).then_inc(s_agg, 1)
                    dve.wait_ge(s_agg, 4 * t + 2)
                    nc.vector.reciprocal(rcnt[:, :], cnt1[:, :]).then_inc(s_agg, 1)
                    dve.wait_ge(s_agg, 4 * t + 3)
                    nc.vector.tensor_scalar(agg_t[:, :], asum[:, 0:FE], rcnt[:, 0:1], None, ALU.mult
                                            ).then_inc(s_agg, 1)
                if part == 1:
                    dve.wait_ge(s_accp, t + 1)
                    nc.vector.tensor_tensor(x1_t[:, :], bank[0][0:TN, 0:D], x_t[:, :], ALU.add).then_inc(s_x1, 1)
                    dve.wait_ge(s_x1, t + 1)
                    nc.vector.bn_stats(bn6[:, :], x1_t[:, :]).then_inc(s_nrm2, 1)
                    dve.wait_ge(s_nrm2, 5 * t + 1)
                    dve.nop(nofuse=True)
                    nc.vector.bn_aggr(mv[:, :], bn6[:, :]).then_inc(s_nrm2, 1)
                    dve.wait_ge(s_nrm2, 5 * t + 2)
                    nc.vector.tensor_scalar(var_eps[:, :], mv[:, 1:2], EPS, None, ALU.add).then_inc(s_nrm2, 1)
                if part == 2:
                    dve.wait_ge(s_std2, t + 1)
                    nc.vector.reciprocal(rstd[:, :], std[:, :]).then_inc(s_nrm2, 1)
                    dve.wait_ge(s_nrm2, 5 * t + 4)
                    nc.vector.scalar_tensor_tensor(nbias[:, :], mv[:, 0:1], -1.0, rstd[:, :], ALU.mult, ALU.mult
                                                   ).then_inc(s_nrm2, 1)
                if part == 3:
                    dve.wait_ge(s_att, t + 1)
                    nc.vector.tensor_tensor(h2[:, :, :], z2[:, :, :],
                                            att[:, :].unsqueeze(1).to_broadcast([P, MH, TN]), ALU.mult
                                            ).then_inc(s_h2, 1)
                if part == 4:
                    dve.wait_ge(s_yt, t + 1)
                    dve.wait_ge(s_yfree, t + 1)
                    nc.vector.tensor_tensor(y_t[:, :], bank[7][0:TN, 0:D], x1_t[:, :], ALU.add).then_inc(s_y, 1)

            def superblock(s, with_net):
                for q in range(NQ):
                    onehots(s, q)
                    if q == NQ - 1:
                        flush(s)
                    if with_net:
                        net(s - LAG, q, s)

            with dve.Fori(0, LAG) as s:
                superblock(s, False)
            with dve.Fori(LAG, NS) as s:
                superblock(s, True)
            with dve.Fori(NS - LAG, NS) as t:
                for part in range(5):
                    net(t, part, NS)


N_WTS = 14
_INS = ['x', 'src', 'dst', 'edge_attr_96', 'edge_type_201', 'L0_gnn_weight', 'L0_gnn_alpha', 'L0_gnn_bias',
        'L1_gnn_W1', 'L1_gnn_b1', 'L1_gnn_W2', 'L1_gnn_b2', 'L1_gnn_Wa', 'L1_gnn_ba',
        'L1_gnn_W3', 'L1_gnn_b3', 'L1_gnn_W4', 'L1_gnn_b4']


def kernel(**inputs):
    import numpy as np
    import concourse.bacc as bacc
    from concourse.bass_utils import run_bass_kernel_spmd as run
    nc = bacc.Bacc("TRN2", target_bir_lowering=False, num_devices=1)
    arrays, args = {}, []
    for name in _INS:
        a = np.ascontiguousarray(inputs[name])
        arrays[f"in_{name}"] = a
        args.append(nc.dram_tensor(f"in_{name}", a.shape, mybir.dt.from_np(a.dtype), kind="ExternalInput").ap())
    out = nc.dram_tensor("out", inputs['x'].shape, mybir.dt.float32, kind="ExternalOutput").ap()
    gnn_program(nc, *args, out)
    r = run(nc, [arrays], core_ids=[0])
    return r.results[0]["out"]
```

```python
import concourse.bass as bass
from concourse import mybir
from contextlib import ExitStack


def gnn_program(nc, x, src, dst, edge_attr_96, edge_type_201, L0_gnn_weight, L0_gnn_alpha, L0_gnn_bias,
                L1_gnn_W1, L1_gnn_b1, L1_gnn_W2, L1_gnn_b2, L1_gnn_Wa, L1_gnn_ba,
                L1_gnn_W3, L1_gnn_b3, L1_gnn_W4, L1_gnn_b4, out):
    fp32, bf16, i32 = mybir.dt.float32, mybir.dt.bfloat16, mybir.dt.int32
    ALU, ACT, AX = mybir.AluOpType, mybir.ActivationFunctionType, mybir.AxisListType
    ds = bass.ds

    N, D = x.shape
    E, FE = edge_attr_96.shape
    R1 = L0_gnn_alpha.shape[0]
    HID = L1_gnn_W1.shape[1]
    T = (E - N) // 2
    P = 128
    J = 25
    Q = 5
    SB = P * J
    NS = E // SB
    NQ = J // Q
    TN = N // NS
    FC = FE + 1
    NT = 99 * P
    W = 128
    WG = 512
    NWG = 25
    AC = NWG * WG
    LAG = 2
    assert NS * SB == E and NS * TN == N and NT >= N + P and AC >= N + W and Q * NQ == J
    MH = HID // P
    ZREP = 9
    ZC = NT // P // ZREP * FC
    assert P * ZREP * ZC == NT * FC
    EPS = 1e-5

    ctx = ExitStack()
    with ctx:
        def sb(name, shape, dt=fp32):
            return ctx.enter_context(nc.sbuf_tensor(name, shape, dt))

        def sem(name):
            return ctx.enter_context(nc.semaphore(name))

        tables = [nc.dram_tensor(f"attr_sums_{k}", (NT, FC), fp32) for k in range(Q)]
        feats_d = nc.dram_tensor("feats_d", (N, D), fp32)
        vswap_d = nc.dram_tensor("vswap_d", (E,), fp32)

        ident = sb("ident", [P, P])
        identb = sb("identb", [P, P], bf16)
        later = sb("later", [P, P])
        iota_f = sb("iota_f", [P, WG])
        spare_row = sb("spare_row", [P, 1])
        alpha_row = sb("alpha_row", [P, R1])
        w0 = sb("w0", [D, D])
        bias0 = sb("bias0", [D, 1])
        w1x = sb("w1x", [P, HID])
        w1a = sb("w1a", [FE, HID])
        w2 = sb("w2", [P, MH, HID])
        wa = sb("wa", [P, MH])
        wab = sb("wab", [P, MH, P])
        w3 = sb("w3", [P, 1 + MH, HID])
        w4 = sb("w4", [P, MH, D])
        b1 = sb("b1", [P, MH])
        b2 = sb("b2", [P, MH])
        b3 = sb("b3", [P, MH])
        b4 = sb("b4", [P, 1])
        ba = sb("ba", [P, 1])

        src_all = sb("src_all", [P, (NS + 1) * J], i32)
        dst_all = sb("dst_all", [P, NS * J], i32)
        v_all = sb("v_all", [P, NS * J])
        type_then_vswap = sb("type_then_vswap", [P, NS * J], i32)
        type_all, vswap_all = type_then_vswap[:, :], type_then_vswap[:, :].bitcast(fp32)
        dstrel_all = sb("dstrel_all", [P, NS * J])
        base_i = sb("base_i", [P, NS], i32)
        tile_end = sb("tile_end", [P, NS])
        late = sb("late", [P, NS])
        over = sb("over", [P, 4])
        worst = sb("worst", [P, 1])
        worst1 = sb("worst1", [1, 1])
        general = sb("general", [1, 1], i32)
        acc = sb("acc", [P, AC])

        attr = sb("attr", [P, J, FC])
        stage = sb("stage", [P, J, FC])
        same = sb("same", [P, Q, P])
        later_n = sb("later_n", [P, J])
        src_i2 = sb("src_i2", [P, 2, J], i32)
        src_hl = sb("src_hl", [P, 2, J], bf16)
        src_f = sb("src_f", [P, J])
        src_off = sb("src_off", [P, J])
        pick = sb("pick", [P, J])
        idx_b = sb("idx_b", [P, J], i32)
        type_f = sb("type_f", [P, J])
        v_t = sb("v_t", [P, J])
        junk = sb("junk", [P, Q, R1], bf16)
        x_t = sb("x_t", [TN, D])
        bn6 = sb("bn6", [TN, 6])
        mv = sb("mv", [TN, 2])
        var_eps = sb("var_eps", [TN, 1])
        std = sb("std", [TN, 1])
        rstd = sb("rstd", [TN, 1])
        nbias = sb("nbias", [TN, 1])
        h_t = sb("h_t", [TN, D])
        hT = sb("hT", [D, TN])
        f_t = sb("f_t", [TN, D])

        gath = sb("gath", [P, J, D])
        onehot = sb("onehot", [P, Q, WG])
        idx_a = sb("idx_a", [P, J], i32)
        rel_t = sb("rel_t", [P, J])
        alp_t = sb("alp_t", [P, J])
        tab_t = sb("tab_t", [TN, Q, FC])
        acc_t = sb("acc_t", [P, TN])
        x1_t = sb("x1_t", [TN, D])
        asum = sb("asum", [TN, FC])
        cnt1 = sb("cnt1", [TN, 1])
        rcnt = sb("rcnt", [TN, 1])
        agg_t = sb("agg_t", [TN, FE])
        aT = sb("aT", [FE, TN])
        z1 = sb("z1", [P, MH, TN])
        z2 = sb("z2", [P, MH, TN])
        att = sb("att", [P, TN])
        h2 = sb("h2", [P, MH, TN])
        z3 = sb("z3", [P, MH, TN])
        yT = sb("yT", [P, TN])
        y_t = sb("y_t", [TN, D])

        bank = [ctx.enter_context(nc.psum_tensor(f"bank{k}", [P, 512], fp32)) for k in range(8)]

        PART_END = {0: 3, 3: Q}

        def ring5(b, k, n):
            return bank[b][:, k * P:k * P + n] if k < 3 else bank[b + 1][:, (k - 3) * P:(k - 3) * P + n]

        s_src = sem("s_src")
        s_types = sem("s_types")
        s_dst = sem("s_dst")
        s_alpha = sem("s_alpha")
        s_wts = sem("s_wts")
        s_zero = sem("s_zero")
        s_zero_rest = sem("s_zero_rest")
        s_const = sem("s_const")
        s_prep = sem("s_prep")
        s_dstrel = sem("s_dstrel")
        s_over = sem("s_over")
        s_worst = sem("s_worst")
        s_wab = sem("s_wab")
        s_general = sem("s_general")
        s_attr = [sem(f"s_attr{q}") for q in range(NQ)]
        s_meta = sem("s_meta")
        s_metaf = sem("s_metaf")
        s_row = sem("s_row")
        s_same = sem("s_same")
        s_sum = sem("s_sum")
        s_stage = sem("s_stage")
        s_pick = sem("s_pick")
        s_idx = sem("s_idx")
        s_tab = [sem(f"s_tab{k}") for k in range(Q)]
        s_type = sem("s_type")
        s_look = sem("s_look")
        s_v = sem("s_v")
        s_vst = sem("s_vst")
        s_x = sem("s_x")
        s_bn = sem("s_bn")
        s_std = sem("s_std")
        s_norm = sem("s_norm")
        s_h = sem("s_h")
        s_hp = sem("s_hp")
        s_hT = sem("s_hT")
        s_fp = sem("s_fp")
        s_f = sem("s_f")
        s_fst = sem("s_fst")
        s_ffree = sem("s_ffree")
        s_vsw = sem("s_vsw")
        s_idxa = sem("s_idxa")
        s_gath = [sem(f"s_gath{j}") for j in range(J)]
        s_alp = sem("s_alp")
        s_oh = sem("s_oh")
        s_mm = sem("s_mm")
        s_flush = sem("s_flush")
        g_oh = sem("g_oh")
        g_mm = sem("g_mm")
        g_rel = sem("g_rel")
        g_flush = sem("g_flush")
        s_tload = sem("s_tload")
        s_acct = sem("s_acct")
        s_accp = sem("s_accp")
        s_x1 = sem("s_x1")
        s_nrm2 = sem("s_nrm2")
        s_std2 = sem("s_std2")
        s_h1 = sem("s_h1")
        s_agg = sem("s_agg")
        s_tp = sem("s_tp")
        s_tT = sem("s_tT")
        s_z1p = sem("s_z1p")
        s_z1 = sem("s_z1")
        s_z2p = sem("s_z2p")
        s_z2 = sem("s_z2")
        s_lp = sem("s_lp")
        s_att = sem("s_att")
        s_h2 = sem("s_h2")
        s_z3p = sem("s_z3p")
        s_z3 = sem("s_z3")
        s_yp = sem("s_yp")
        s_yT = sem("s_yT")
        s_yt = sem("s_yt")
        s_y = sem("s_y")
        s_out = sem("s_out")
        s_yfree = sem("s_yfree")

        block = ctx.enter_context(nc.Block())

        @block.sync
        def _(sp):
            v = lambda a: a.rearrange("(s p j) -> p s j", p=P, j=J)
            all3 = lambda t: t.rearrange("p (s j) -> p s j", j=J)
            sp.dma_start(all3(src_all[:, 0:NS * J]), v(src)).then_inc(s_src, 16)
            sp.dma_start(all3(type_all), v(edge_type_201)).then_inc(s_types, 16)
            attr_v = edge_attr_96.rearrange("(s p j) f -> s p j f", p=P, j=J)
            x_v = x.rearrange("(t n) f -> t n f", n=TN)
            feats_v = feats_d.rearrange("(t n) f -> t n f", n=TN)

            def loads_b(s, first=False):
                for q in range(NQ):
                    if not first:
                        sp.wait_ge(s_sum, J + J * (s - 1) + Q * (q + 1))
                    sp.dma_start(attr[:, q * Q:(q + 1) * Q, 0:FE], attr_v[ds(s, 1), :, q * Q:(q + 1) * Q, :].rearrange(
                        "o p j f -> (o p) j f")).then_inc(s_attr[q], 16)
                    if q == 0:
                        sp.wait_ge(s_h, 1 + s)
                        sp.dma_start(x_t[:, :], x_v[ds(s, 1), :, :].rearrange("o n f -> (o n) f")).then_inc(s_x, 16)

            def store_f(s):
                sp.wait_ge(s_f, s + 2)
                sp.dma_start(feats_v[ds(s, 1), :, :].rearrange("o n f -> (o n) f"), f_t[:, :]).then_inc(s_fst, 16)
                sp.wait_ge(s_fst, 16 * (s + 1))
                sp.sem_inc(s_ffree, 1)

            def store_v(s, p0, p1, shift):
                sp.wait_ge(s_v, s + 1)
                dest = vswap_d[ds(s * SB + p0 * J + shift, (p1 - p0) * J)].rearrange("(p j) -> p j", j=J)
                sp.dma_start(dest, v_all[p0:p1, ds(s * J, J)]).then_inc(s_vst, 16)

            sp.sem_inc(s_ffree, 1)
            sp.wait_ge(s_h, 1)
            loads_b(0, first=True)
            cut1, cut2 = T // SB, 2 * T // SB
            pc1, pc2 = (T - cut1 * SB) // J, (2 * T - cut2 * SB) // J
            assert cut1 * SB + pc1 * J == T and cut2 * SB + pc2 * J == 2 * T
            spans = [(0, cut1, [(0, P, T)]), (cut1, cut1 + 1, [(0, pc1, T), (pc1, P, -T)]),
                     (cut1 + 1, cut2, [(0, P, -T)]), (cut2, cut2 + 1, [(0, pc2, -T), (pc2, P, 0)]),
                     (cut2 + 1, NS, [(0, P, 0)])]
            n_vst = 0
            for lo, hi, parts in spans:
                n_vst += (hi - lo) * len(parts)
                with sp.Fori(lo, hi if hi < NS else NS - 1) as s:
                    loads_b(s + 1)
                    store_f(s)
                    for p0, p1, shift in parts:
                        store_v(s, p0, p1, shift)
                if lo:
                    continue
                sp.dma_start(all3(dst_all[:, :]), v(dst)).then_inc(s_dst, 16)
                with nc.allow_non_contiguous_dma(reason="one index per superblock"):
                    sp.dma_start(base_i[:, :], bass.AP(dst.tensor, 0, [[0, P], [SB, NS], [1, 1]])).then_inc(s_dst, 16)
            store_f(NS - 1)
            store_v(NS - 1, 0, P, 0)

            sp.wait_ge(s_vst, 16 * n_vst)
            sp.dma_start(all3(vswap_all), v(vswap_d)).then_inc(s_vsw, 16)
            for k in range(Q):
                sp.wait_ge(s_tab[k], 16 + 16 * NS * NQ)
            sp.sem_inc(s_yfree, 1)

            def load_a(t):
                sp.dma_start(x_t[:, :], x_v[ds(t, 1), :, :].rearrange("o n f -> (o n) f")).then_inc(s_tload, 16)
                for k in range(Q):
                    sp.dma_start(tab_t[:, k, :], tables[k][ds(t * TN, TN), :]).then_inc(s_tload, 16)

            def store_y(t):
                sp.wait_ge(s_y, t + 1)
                sp.dma_start(out[ds(t * TN, TN), :], y_t[:, :]).then_inc(s_out, 16)
                sp.wait_ge(s_out, 16 * (t + 1))
                sp.sem_inc(s_yfree, 1)

            load_a(0)
            with sp.Fori(0, NS - 1) as t:
                sp.wait_ge(s_x1, t + 1)
                load_a(t + 1)
                store_y(t)
            store_y(NS - 1)
            sp.wait_ge(s_out, 16 * NS)

        @block.gpsimd
        def _(gp):
            gp.memset(ident[:, :], 0.0).then_inc(s_const, 1)
            gp.memset(later[:, :], 1.0).then_inc(s_const, 1)
            gp.wait_ge(s_const, 2)
            gp.affine_select(out=ident[:, :], in_=ident[:, :], compare_op=ALU.not_equal, fill=1.0, base=0,
                             pattern=[[-1, P]], channel_multiplier=1).then_inc(s_const, 1)
            gp.affine_select(out=later[:, :], in_=later[:, :], compare_op=ALU.is_ge, fill=0.0, base=0,
                             pattern=[[1, P]], channel_multiplier=-1).then_inc(s_const, 1)
            gp.iota(iota_f[:, :], pattern=[[1, WG]], base=0, channel_multiplier=0,
                    allow_small_or_imprecise_dtypes=True).then_inc(s_const, 1)
            gp.iota(spare_row[:, :], pattern=[[0, 1]], base=N, channel_multiplier=1,
                    allow_small_or_imprecise_dtypes=True).then_inc(s_const, 1)

            gp.wait_ge(s_zero, 1)
            for k in range(Q):
                gp.dma_start(tables[k].rearrange("(p r a) f -> p r (a f)", p=P, r=ZREP),
                             acc[:, 0:ZC].unsqueeze(1).to_broadcast([P, ZREP, ZC])).then_inc(s_tab[k], 16)
            gp.memset(acc[:, ZC:AC], 0.0).then_inc(s_zero_rest, 1)
            gp.iota(tile_end[:, :], pattern=[[TN, NS]], base=TN * (1 - LAG), channel_multiplier=0,
                    allow_small_or_imprecise_dtypes=True).then_inc(s_const, 1)

            with gp.Fori(0, NS) as s:
                for q in range(NQ):
                    gp.wait_ge(s_idx, NQ * s + q + 1)
                    gp.nop(nofuse=True)
                    for k in range(Q):
                        j = q * Q + k
                        gp.wait_ge(s_tab[k], 16 + 16 * (NQ * s + q))
                        gp.nop(nofuse=True)
                        gp.indirect_dma_start(tables[k][:, :], bass.IndirectOffsetOnAxis(ap=idx_b[:, j:j + 1], axis=0),
                                              stage[:, j, :], None, compute_op=ALU.add).then_inc(s_tab[k], 16)
            gp.wait_ge(s_fst, 16 * NS)
            gp.nop(nofuse=True)
            with gp.Fori(0, NS) as s:
                for q in range(NQ):
                    gp.wait_ge(s_idxa, NQ * s + q + 1)
                    gp.nop(nofuse=True)
                    for k in range(Q):
                        j = q * Q + k
                        gp.indirect_dma_start(gath[:, j, :], None, feats_d[:, :],
                                              bass.IndirectOffsetOnAxis(ap=idx_a[:, j:j + 1], axis=0)
                                              ).then_inc(s_gath[j], 16)

        @block.tensor
        def _(pe):
            pe.sem_inc(s_sum, J)
            pe.sem_inc(s_mm, J)
            pe.wait_ge(s_prep, 1)

            def rows(s, q):
                for k in range(Q):
                    j = q * Q + k
                    if j == 0:
                        pe.wait_ge(s_meta, s + 1)
                    if k in PART_END:
                        pe.wait_ge(s_same, J * s + q * Q + PART_END[k])
                    for half in range(2):
                        last = nc.tensor.matmul(ring5(0, k, P), src_hl[:, half, j:j + 1].to_broadcast([P, P]),
                                                identb[:, :], start=half == 0, stop=half == 1)
                    last.then_inc(s_row, 1)

            rows(0, 0)
            with pe.Fori(0, NS) as s:
                for q in range(NQ):
                    pe.wait_ge(s_attr[q], 16 * (s + 1))
                    for k in range(Q):
                        j = q * Q + k
                        pe.wait_ge(s_same, Q + J * s + j + 1)
                        if k in PART_END:
                            pe.wait_ge(s_stage, J * s + q * Q + PART_END[k])
                        ps = ring5(2, k, FC)
                        nc.tensor.matmul(ps, same[:, k, :], attr[:, j, :], start=True, stop=True).then_inc(s_sum, 1)
                    if q < NQ - 1:
                        rows(s, q + 1)
                    else:
                        rows(s + 1, 0)
                    if q == 2:
                        pe.wait_ge(s_h, s + 2)
                        nc.tensor.transpose(bank[5][:, 0:TN], h_t[:, :], ident[0:TN, 0:TN]).then_inc(s_hp, 1)
                    if q == 3:
                        pe.wait_ge(s_hT, s + 1)
                        pe.wait_ge(s_wts, 16 * N_WTS)
                        pe.wait_ge(s_f, s + 1)
                        nc.tensor.matmul(bank[6][0:TN, 0:D], hT[:, :], w0[:, :], start=True, stop=True
                                         ).then_inc(s_fp, 1)

            def sums(s, q):
                for k in range(Q):
                    j = q * Q + k
                    if j == 0:
                        pe.wait_ge(s_flush, s + 1)
                    pe.wait_ge(s_gath[j], 16 * (s + 1))
                    pe.wait_ge(s_oh, J * s + j + 1)
                    nc.tensor.matmul(bank[4][:, 0:W], gath[:, j, :], onehot[:, k, 0:W],
                                     start=j == 0, stop=j == J - 1).then_inc(s_mm, 1)

            def net(t, part):
                if part == 0:
                    pe.wait_ge(s_acct, t + 1)
                    nc.tensor.transpose(bank[0][0:TN, 0:D], acc_t[:, :], ident[:, :]).then_inc(s_accp, 1)
                if part == 1:
                    pe.wait_ge(s_h1, t + 1)
                    nc.tensor.transpose(bank[0][:, 128:128 + TN], h_t[:, :], ident[0:TN, 0:TN])
                    pe.wait_ge(s_agg, 4 * (t + 1))
                    nc.tensor.transpose(bank[0][0:FE, 256:256 + TN], agg_t[:, :], ident[0:TN, 0:TN]).then_inc(s_tp, 1)
                    pe.wait_ge(s_tT, 2 * (t + 1))
                    for m in range(MH):
                        col = slice(m * P, (m + 1) * P)
                        nc.tensor.matmul(bank[1][:, m * P:m * P + TN], w1x[:, col], hT[:, :], start=True, stop=False)
                        last = nc.tensor.matmul(bank[1][:, m * P:m * P + TN], w1a[:, col], aT[:, :],
                                                start=False, stop=True)
                    last.then_inc(s_z1p, 1)
                if part == 2:
                    pe.wait_ge(s_z1, MH * (t + 1))
                    for m in range(MH):
                        for c in range(MH):
                            last = nc.tensor.matmul(bank[2][:, m * P:m * P + TN], w2[:, c, m * P:(m + 1) * P],
                                                    z1[:, c, :], start=c == 0, stop=c == MH - 1)
                    last.then_inc(s_z2p, 1)
                    pe.wait_ge(s_z2, MH * (t + 1))
                    for c in range(MH):
                        last = nc.tensor.matmul(bank[3][:, 0:TN], wab[:, c, :], z2[:, c, :],
                                                start=c == 0, stop=c == MH - 1)
                    last.then_inc(s_lp, 1)
                if part == 3:
                    pe.wait_ge(s_h2, t + 1)
                    for m in range(MH):
                        for c in range(1 + MH):
                            last = nc.tensor.matmul(bank[5][:, m * P:m * P + TN], w3[:, c, m * P:(m + 1) * P],
                                                    hT[:, :] if c == 0 else h2[:, c - 1, :],
                                                    start=c == 0, stop=c == MH)
                    last.then_inc(s_z3p, 1)
                    pe.wait_ge(s_z3, MH * (t + 1))
                    for c in range(MH):
                        last = nc.tensor.matmul(bank[6][:, 0:TN], w4[:, c, :], z3[:, c, :],
                                                start=c == 0, stop=c == MH - 1)
                    last.then_inc(s_yp, 1)
                if part == 4:
                    pe.wait_ge(s_yT, t + 1)
                    nc.tensor.transpose(bank[7][0:TN, 0:D], yT[:, :], ident[:, :]).then_inc(s_yt, 1)

            def superblock(s, with_net):
                for q in range(NQ):
                    sums(s, q)
                    if with_net:
                        net(s - LAG, q)

            def sums_general(s, w):
                n = s * NWG + w
                pe.wait_ge(g_flush, n + 1)
                for q in range(NQ):
                    pe.wait_ge(g_oh, n * NQ + q + 1)
                    for k in range(Q):
                        j = q * Q + k
                        last = nc.tensor.matmul(bank[4][:, 0:WG], gath[:, j, :], onehot[:, k, :],
                                                start=j == 0, stop=j == J - 1)
                    last.then_inc(g_mm, 1)

            pe.wait_ge(s_over, 6)
            nc.tensor.matmul(bank[7][0:1, 0:P], worst[:, :], ident[:, :], start=True, stop=True).then_inc(s_worst, 1)
            pe.wait_ge(s_wab, MH)
            pe.wait_ge(s_general, 1)
            flag = pe.value_load(general[0:1, 0:1], min_val=0, max_val=1)
            with pe.If(flag):
                with pe.Fori(0, NS) as s:
                    for j in range(J):
                        pe.wait_ge(s_gath[j], 16 * (s + 1))
                    pe.nop(nofuse=True)
                    with pe.Fori(0, NWG) as w:
                        sums_general(s, w)
                with pe.Fori(0, NS) as t:
                    for part in range(5):
                        net(t, part)
            with pe.Else():
                with pe.Fori(0, LAG) as s:
                    superblock(s, False)
                with pe.Fori(LAG, NS) as s:
                    superblock(s, True)
                with pe.Fori(NS - LAG, NS) as t:
                    for part in range(5):
                        net(t, part)

        @block.scalar
        def _(act):
            act.sem_inc(s_h, 1)
            act.sem_inc(s_f, 1)
            act.sem_inc(s_stage, Q)
            with nc.allow_non_contiguous_dma(reason="small parameter columns"):
                act.dma_start(alpha_row[:, :], bass.AP(L0_gnn_alpha.tensor, 0, [[0, P], [1, R1]])).then_inc(s_alpha, 16)
                act.dma_start(w0[:, :], L0_gnn_weight).then_inc(s_wts, 16)
                act.dma_start(bias0[:, :], L0_gnn_bias.rearrange("(p o) -> p o", o=1)).then_inc(s_wts, 16)
                act.dma_start(w1x[:, :], L1_gnn_W1[0:D, :]).then_inc(s_wts, 16)
                act.dma_start(w1a[:, :], L1_gnn_W1[D:D + FE, :]).then_inc(s_wts, 16)
                act.dma_start(w2[:, :, :], L1_gnn_W2.rearrange("(c p) n -> p c n", p=P)).then_inc(s_wts, 16)
                act.dma_start(w3[:, :, :], L1_gnn_W3.rearrange("(c p) n -> p c n", p=P)).then_inc(s_wts, 16)
                act.dma_start(w4[:, :, :], L1_gnn_W4.rearrange("(c p) n -> p c n", p=P)).then_inc(s_wts, 16)
                act.dma_start(wa[:, :], L1_gnn_Wa.rearrange("(c p) o -> p (c o)", p=P)).then_inc(s_wts, 16)
                act.dma_start(b1[:, :], L1_gnn_b1.rearrange("(c p) -> p c", p=P)).then_inc(s_wts, 16)
                act.dma_start(b2[:, :], L1_gnn_b2.rearrange("(c p) -> p c", p=P)).then_inc(s_wts, 16)
                act.dma_start(b3[:, :], L1_gnn_b3.rearrange("(c p) -> p c", p=P)).then_inc(s_wts, 16)
                act.dma_start(b4[:, :], L1_gnn_b4.rearrange("(p o) -> p o", o=1)).then_inc(s_wts, 16)
                act.dma_start(ba[:, :], bass.AP(L1_gnn_ba.tensor, 0, [[0, P], [1, 1]])).then_inc(s_wts, 16)

            def stages(s, first=False):
                for q in range(NQ):
                    for k in range(Q):
                        j = q * Q + k
                        if k in PART_END:
                            act.wait_ge(s_sum, J + J * s + q * Q + PART_END[k])
                        if not first:
                            act.wait_ge(s_tab[k], 16 + 16 * (NQ * (s - 1) + q + 1))
                        nc.scalar.activation(stage[:, j, :], ring5(2, k, FC), ACT.Copy).then_inc(s_stage, 1)
                    if q == 0:
                        act.wait_ge(s_bn, 4 * s + 3)
                        nc.scalar.activation(std[:, :], var_eps[:, :], ACT.Sqrt).then_inc(s_std, 1)
                    if q == 1:
                        act.wait_ge(s_norm, s + 1)
                        nc.scalar.activation(h_t[:, :], x_t[:, :], ACT.Relu, bias=nbias[:, :], scale=rstd[:, :]
                                             ).then_inc(s_h, 1)
                    if q == 2:
                        act.wait_ge(s_hp, s + 1)
                        nc.scalar.activation(hT[:, :], bank[5][:, 0:TN], ACT.Copy).then_inc(s_hT, 1)
                    if q == 4:
                        act.wait_ge(s_fp, s + 1)
                        act.wait_ge(s_ffree, s + 1)
                        nc.scalar.activation(f_t[:, :], bank[6][0:TN, 0:D], ACT.Copy).then_inc(s_f, 1)

            stages(0, first=True)
            with act.Fori(1, NS) as s:
                stages(s)
            act.wait_ge(s_wts, 16 * N_WTS)

            def indices(s, q):
                act.wait_ge(s_mm, J * s + Q * (q + 1))
                nc.scalar.activation(idx_a[:, q * Q:(q + 1) * Q], src_all[:, ds(s * J + q * Q, Q)], ACT.Copy
                                     ).then_inc(s_idxa, 1)

            def net(t, between=lambda q: None):
                between(0)
                act.wait_ge(s_nrm2, 5 * t + 3)
                nc.scalar.activation(std[:, :], var_eps[:, :], ACT.Sqrt).then_inc(s_std2, 1)
                act.wait_ge(s_nrm2, 5 * (t + 1))
                nc.scalar.activation(h_t[:, :], x1_t[:, :], ACT.Relu, bias=nbias[:, :], scale=rstd[:, :]
                                     ).then_inc(s_h1, 1)
                act.wait_ge(s_tp, t + 1)
                nc.scalar.activation(hT[:, :], bank[0][:, 128:128 + TN], ACT.Copy).then_inc(s_tT, 1)
                nc.scalar.activation(aT[:, :], bank[0][0:FE, 256:256 + TN], ACT.Copy).then_inc(s_tT, 1)
                between(1)
                act.wait_ge(s_z1p, t + 1)
                for m in range(MH):
                    nc.scalar.activation(z1[:, m, :], bank[1][:, m * P:m * P + TN], ACT.Relu, bias=b1[:, m:m + 1]
                                         ).then_inc(s_z1, 1)
                between(2)
                act.wait_ge(s_z2p, t + 1)
                for m in range(MH):
                    nc.scalar.activation(z2[:, m, :], bank[2][:, m * P:m * P + TN], ACT.Identity, bias=b2[:, m:m + 1]
                                         ).then_inc(s_z2, 1)
                act.wait_ge(s_lp, t + 1)
                nc.scalar.activation(att[:, :], bank[3][:, 0:TN], ACT.Sigmoid, bias=ba[:, :]).then_inc(s_att, 1)
                between(3)
                act.wait_ge(s_z3p, t + 1)
                for m in range(MH):
                    nc.scalar.activation(z3[:, m, :], bank[5][:, m * P:m * P + TN], ACT.Relu, bias=b3[:, m:m + 1]
                                         ).then_inc(s_z3, 1)
                act.wait_ge(s_yp, t + 1)
                nc.scalar.activation(yT[:, :], bank[6][:, 0:TN], ACT.Identity, bias=b4[:, :]).then_inc(s_yT, 1)
                between(4)

            for q in range(NQ):
                indices(0, q)
            act.wait_ge(s_general, 1)
            flag = act.value_load(general[0:1, 0:1], min_val=0, max_val=1)
            with act.If(flag):
                with act.Fori(1, NS) as s:
                    for q in range(NQ):
                        indices(s, q)
                with act.Fori(0, NS) as t:
                    net(t)
            with act.Else():
                with act.Fori(0, LAG) as s:
                    for q in range(NQ):
                        indices(s + 1, q)
                with act.Fori(LAG, NS) as s:
                    net(s - LAG, lambda q: indices(s + 1, q))
                with act.Fori(NS - LAG, NS) as t:
                    net(t)

        @block.vector
        def _(dve):
            dve.sem_inc(s_same, Q)
            dve.sem_inc(s_flush, 1)
            nc.vector.memset(acc[:, 0:ZC], 0.0).then_inc(s_zero, 1)
            nc.vector.memset(attr[:, :, FE:FC], 1.0)
            nc.vector.memset(src_all[:, NS * J:(NS + 1) * J], 0)
            dve.wait_ge(s_const, 6)
            nc.vector.tensor_copy(identb[:, :], ident[:, :]).then_inc(s_prep, 1)
            dve.wait_ge(s_src, 16)

            def convert_src(s, first=False):
                nc.vector.tensor_scalar(src_i2[:, 0, :], src_all[:, ds(s * J, J)], 0x7F80, None, ALU.bitwise_and
                                        ).then_inc(s_metaf, 1)
                nc.vector.tensor_scalar(src_i2[:, 1, :], src_all[:, ds(s * J, J)], 0x7F, None, ALU.bitwise_and
                                        ).then_inc(s_metaf, 1)
                if not first:
                    dve.wait_ge(s_same, Q + J * s)
                    dve.nop(nofuse=True)
                nc.vector.tensor_copy(src_f[:, :], src_all[:, ds(s * J, J)]).then_inc(s_metaf, 1)
                dve.wait_ge(s_metaf, 3 * s + 3)
                nc.vector.tensor_copy(src_hl[:, :, :], src_i2[:, :, :]).then_inc(s_meta, 1)

            convert_src(0, first=True)
            dve.wait_ge(s_alpha, 16)
            nc.vector.memset(alpha_row[:, 0:1], 0.0).then_inc(s_look, 1)
            dve.wait_ge(s_types, 16)
            with dve.Fori(0, NS) as s:
                nc.vector.tensor_copy(type_f[:, :], type_all[:, ds(s * J, J)]).then_inc(s_type, 1)
                nc.vector.tensor_scalar(src_off[:, :], src_f[:, :], spare_row[:, 0:1], None, ALU.subtract
                                        ).then_inc(s_pick, 1)
                for q in range(NQ):
                    group = slice(q * Q, (q + 1) * Q)
                    for k in range(Q):
                        j = q * Q + k
                        if k in PART_END:
                            dve.wait_ge(s_row, J * s + q * Q + PART_END[k])
                        dve.wait_ge(s_sum, J - Q + J * s + j + 1)
                        nc.vector.scalar_tensor_tensor(same[:, k, :], ring5(0, k, P), src_f[:, j:j + 1],
                                                       later[:, :], ALU.is_equal, ALU.mult,
                                                       accum_out=later_n[:, j:j + 1]).then_inc(s_same, 1)
                    if q == NQ - 1:
                        convert_src(s + 1)
                    for k in range(Q):
                        j = q * Q + k
                        if j == 0:
                            dve.wait_ge(s_type, s + 1)
                        if k == 0:
                            dve.wait_ge(s_look, NQ * s + q + 1)
                        last = nc.vector.scalar_tensor_tensor(junk[:, k, :], iota_f[:, 0:R1], type_f[:, j:j + 1],
                                                              alpha_row[:, :], ALU.is_equal, ALU.mult,
                                                              accum_out=v_t[:, j:j + 1])
                    last.then_inc(s_look, 1)
                    dve.wait_ge(s_same, Q + J * s + Q * (q + 1))
                    dve.wait_ge(s_pick, (NQ + 1) * s + q + 1)
                    nc.vector.scalar_tensor_tensor(pick[:, group], later_n[:, group], 1.0, src_off[:, group],
                                                   ALU.is_equal, ALU.mult).then_inc(s_pick, 1)
                    dve.wait_ge(s_pick, (NQ + 1) * s + q + 2)
                    dve.wait_ge(s_stage, Q + J * s + Q * (q + 1))
                    nc.vector.tensor_scalar(idx_b[:, group], pick[:, group], spare_row[:, 0:1], None, ALU.add
                                            ).then_inc(s_idx, 1)
                    if q == 0:
                        dve.wait_ge(s_x, 16 * (s + 1))
                        nc.vector.bn_stats(bn6[:, :], x_t[:, :]).then_inc(s_bn, 1)
                        dve.wait_ge(s_bn, 4 * s + 1)
                        dve.nop(nofuse=True)
                        nc.vector.bn_aggr(mv[:, :], bn6[:, :]).then_inc(s_bn, 1)
                        dve.wait_ge(s_bn, 4 * s + 2)
                        nc.vector.tensor_scalar(var_eps[:, :], mv[:, 1:2], EPS, None, ALU.add).then_inc(s_bn, 1)
                    if q == 1:
                        dve.wait_ge(s_std, s + 1)
                        nc.vector.reciprocal(rstd[:, :], std[:, :]).then_inc(s_bn, 1)
                        dve.wait_ge(s_bn, 4 * s + 4)
                        nc.vector.scalar_tensor_tensor(nbias[:, :], mv[:, 0:1], -1.0, rstd[:, :], ALU.mult, ALU.mult
                                                       ).then_inc(s_norm, 1)
                dve.wait_ge(s_look, NQ * (s + 1) + 1)
                nc.vector.tensor_copy(v_all[:, ds(s * J, J)], v_t[:, :]).then_inc(s_v, 1)

            dve.wait_ge(s_wts, 16 * N_WTS)
            for c in range(MH):
                nc.vector.tensor_copy(wab[:, c, :], wa[:, c:c + 1].to_broadcast([P, P])).then_inc(s_wab, 1)
            dve.wait_ge(s_const, 7)
            dve.wait_ge(s_dst, 32)
            nc.vector.tensor_tensor(dstrel_all[:, :].rearrange("p (s j) -> p s j", j=J),
                                    dst_all[:, :].rearrange("p (s j) -> p s j", j=J),
                                    base_i[:, :].unsqueeze(2).to_broadcast([P, NS, J]), ALU.subtract
                                    ).then_inc(s_dstrel, 1)
            dve.wait_ge(s_dstrel, 1)
            nc.vector.tensor_reduce(over[:, 0:1], dstrel_all[:, :], AX.X, ALU.max).then_inc(s_over, 1)
            nc.vector.tensor_reduce(over[:, 1:2], dstrel_all[:, :], AX.X, ALU.min, negate=True).then_inc(s_over, 1)
            nc.vector.tensor_tensor(late[:, :], tile_end[:, :], base_i[:, :], ALU.subtract).then_inc(s_over, 1)
            dve.wait_ge(s_over, 3)
            nc.vector.tensor_reduce(over[:, 2:3], late[:, :], AX.X, ALU.max).then_inc(s_over, 1)
            nc.vector.tensor_scalar(over[:, 3:4], over[:, 0:1], float(1 - W), None, ALU.add).then_inc(s_over, 1)
            dve.wait_ge(s_over, 5)
            nc.vector.tensor_reduce(worst[:, :], over[:, 1:4], AX.X, ALU.max).then_inc(s_over, 1)
            dve.wait_ge(s_worst, 1)
            nc.vector.tensor_reduce(worst1[:, :], bank[7][0:1, 0:P], AX.X, ALU.max).then_inc(s_over, 1)
            dve.wait_ge(s_over, 7)
            nc.vector.tensor_scalar(general[:, :], worst1[:, :], 0.0, None, ALU.is_gt).then_inc(s_general, 1)
            dve.wait_ge(s_zero_rest, 1)
            dve.wait_ge(s_vsw, 16)

            def onehots(s, q):
                if q == 0:
                    nc.vector.tensor_copy(rel_t[:, :], dstrel_all[:, ds(s * J, J)]).then_inc(s_alp, 1)
                    nc.vector.tensor_tensor(alp_t[:, :], v_all[:, ds(s * J, J)], vswap_all[:, ds(s * J, J)], ALU.add
                                            ).then_inc(s_alp, 1)
                    dve.wait_ge(s_alp, 2 * (s + 1))
                for k in range(Q):
                    j = q * Q + k
                    dve.wait_ge(s_mm, J - Q + J * s + j + 1)
                    nc.vector.tensor_scalar(onehot[:, k, 0:W], iota_f[:, 0:W], rel_t[:, j:j + 1], alp_t[:, j:j + 1],
                                            ALU.is_equal, ALU.mult).then_inc(s_oh, 1)

            def flush(s):
                dve.wait_ge(s_mm, J + J * (s + 1))
                base = dve.value_load(base_i[0:1, ds(s, 1)], min_val=0, max_val=N - 1)
                nc.vector.tensor_tensor(acc[:, ds(base, W)], acc[:, ds(base, W)], bank[4][:, 0:W], ALU.add
                                        ).then_inc(s_flush, 1)

            def net(t, part, flushes, count):
                if part == 0:
                    dve.wait_ge(flushes, count + 1)
                    nc.vector.tensor_scalar(acc_t[:, :], acc[:, ds(t * TN, TN)], bias0[:, 0:1], None, ALU.add
                                            ).then_inc(s_acct, 1)
                    dve.wait_ge(s_tload, 16 * (Q + 1) * (t + 1))
                    nc.vector.tensor_reduce(asum[:, :], tab_t[:, :, :].rearrange("p k f -> p f k"), AX.X, ALU.add
                                            ).then_inc(s_agg, 1)
                    dve.wait_ge(s_agg, 4 * t + 1)
                    nc.vector.tensor_scalar(cnt1[:, :], asum[:, FE:FC], 1.0, None, ALU.max).then_inc(s_agg, 1)
                    dve.wait_ge(s_agg, 4 * t + 2)
                    nc.vector.reciprocal(rcnt[:, :], cnt1[:, :]).then_inc(s_agg, 1)
                    dve.wait_ge(s_agg, 4 * t + 3)
                    nc.vector.tensor_scalar(agg_t[:, :], asum[:, 0:FE], rcnt[:, 0:1], None, ALU.mult
                                            ).then_inc(s_agg, 1)
                if part == 1:
                    dve.wait_ge(s_accp, t + 1)
                    nc.vector.tensor_tensor(x1_t[:, :], bank[0][0:TN, 0:D], x_t[:, :], ALU.add).then_inc(s_x1, 1)
                    dve.wait_ge(s_x1, t + 1)
                    nc.vector.bn_stats(bn6[:, :], x1_t[:, :]).then_inc(s_nrm2, 1)
                    dve.wait_ge(s_nrm2, 5 * t + 1)
                    dve.nop(nofuse=True)
                    nc.vector.bn_aggr(mv[:, :], bn6[:, :]).then_inc(s_nrm2, 1)
                    dve.wait_ge(s_nrm2, 5 * t + 2)
                    nc.vector.tensor_scalar(var_eps[:, :], mv[:, 1:2], EPS, None, ALU.add).then_inc(s_nrm2, 1)
                if part == 2:
                    dve.wait_ge(s_std2, t + 1)
                    nc.vector.reciprocal(rstd[:, :], std[:, :]).then_inc(s_nrm2, 1)
                    dve.wait_ge(s_nrm2, 5 * t + 4)
                    nc.vector.scalar_tensor_tensor(nbias[:, :], mv[:, 0:1], -1.0, rstd[:, :], ALU.mult, ALU.mult
                                                   ).then_inc(s_nrm2, 1)
                if part == 3:
                    dve.wait_ge(s_att, t + 1)
                    nc.vector.tensor_tensor(h2[:, :, :], z2[:, :, :],
                                            att[:, :].unsqueeze(1).to_broadcast([P, MH, TN]), ALU.mult
                                            ).then_inc(s_h2, 1)
                if part == 4:
                    dve.wait_ge(s_yt, t + 1)
                    dve.wait_ge(s_yfree, t + 1)
                    nc.vector.tensor_tensor(y_t[:, :], bank[7][0:TN, 0:D], x1_t[:, :], ALU.add).then_inc(s_y, 1)

            def superblock(s, with_net):
                for q in range(NQ):
                    onehots(s, q)
                    if q == NQ - 1:
                        flush(s)
                    if with_net:
                        net(s - LAG, q, s_flush, s)

            def window_general(s, w):
                n = s * NWG + w
                for q in range(NQ):
                    dve.wait_ge(g_mm, n * NQ + q + 1)
                    for k in range(Q):
                        j = q * Q + k
                        last = nc.vector.tensor_scalar(onehot[:, k, :], iota_f[:, :], rel_t[:, j:j + 1],
                                                       alp_t[:, j:j + 1], ALU.is_equal, ALU.mult)
                    last.then_inc(g_oh, 1)
                dve.wait_ge(g_mm, (n + 1) * NQ + 1)
                nc.vector.tensor_scalar(rel_t[:, :], rel_t[:, :], float(-WG), None, ALU.add).then_inc(g_rel, 1)
                dve.wait_ge(g_rel, (NWG + 3) * s + w + 4)
                nc.vector.tensor_tensor(acc[:, ds(w * WG, WG)], acc[:, ds(w * WG, WG)], bank[4][:, 0:WG], ALU.add
                                        ).then_inc(g_flush, 1)

            dve.wait_ge(s_general, 1)
            flag = dve.value_load(general[0:1, 0:1], min_val=0, max_val=1)
            with dve.If(flag):
                dve.sem_inc(g_flush, 1)
                dve.sem_inc(g_mm, 1)
                with dve.Fori(0, NS) as s:
                    nc.vector.tensor_copy(rel_t[:, :], dstrel_all[:, ds(s * J, J)]).then_inc(g_rel, 1)
                    nc.vector.tensor_tensor(alp_t[:, :], v_all[:, ds(s * J, J)], vswap_all[:, ds(s * J, J)], ALU.add
                                            ).then_inc(g_rel, 1)
                    dve.wait_ge(g_rel, (NWG + 3) * s + 2)
                    nc.vector.tensor_tensor(rel_t[:, :], rel_t[:, :], base_i[:, ds(s, 1)].to_broadcast([P, J]), ALU.add
                                            ).then_inc(g_rel, 1)
                    dve.wait_ge(g_rel, (NWG + 3) * s + 3)
                    dve.nop(nofuse=True)
                    with dve.Fori(0, NWG) as w:
                        window_general(s, w)
                    dve.sem_inc(s_mm, J)
                with dve.Fori(0, NS) as t:
                    for part in range(5):
                        net(t, part, g_flush, NS * NWG)
            with dve.Else():
                with dve.Fori(0, LAG) as s:
                    superblock(s, False)
                with dve.Fori(LAG, NS) as s:
                    superblock(s, True)
                with dve.Fori(NS - LAG, NS) as t:
                    for part in range(5):
                        net(t, part, s_flush, NS)


N_WTS = 13
_INS = ['x', 'src', 'dst', 'edge_attr_96', 'edge_type_201', 'L0_gnn_weight', 'L0_gnn_alpha', 'L0_gnn_bias',
        'L1_gnn_W1', 'L1_gnn_b1', 'L1_gnn_W2', 'L1_gnn_b2', 'L1_gnn_Wa', 'L1_gnn_ba',
        'L1_gnn_W3', 'L1_gnn_b3', 'L1_gnn_W4', 'L1_gnn_b4']


def kernel(**inputs):
    import numpy as np
    import concourse.bacc as bacc
    from concourse.bass_utils import run_bass_kernel_spmd as run
    nc = bacc.Bacc("TRN2", target_bir_lowering=False, num_devices=1)
    arrays, args = {}, []
    for name in _INS:
        a = np.ascontiguousarray(inputs[name])
        arrays[f"in_{name}"] = a
        args.append(nc.dram_tensor(f"in_{name}", a.shape, mybir.dt.from_np(a.dtype), kind="ExternalInput").ap())
    out = nc.dram_tensor("out", inputs['x'].shape, mybir.dt.float32, kind="ExternalOutput").ap()
    gnn_program(nc, *args, out)
    r = run(nc, [arrays], core_ids=[0])
    return r.results[0]["out"]
```
